# Optimizing a Trainium2 kernel written in Bass

```python
import numpy as np
import jax
import jax.numpy as jnp

def _softmax(x, axis=-1):
    return jax.nn.softmax(x, axis=axis)

def _gelu(x):
    return jax.nn.gelu(x, approximate=True)

def _silu(x):
    return jax.nn.silu(x)

def _sigmoid(x):
    return jax.nn.sigmoid(x)

def _layernorm(x, axis=-1, eps=1e-05):
    m = jnp.mean(x, axis=axis, keepdims=True)
    v = jnp.var(x, axis=axis, keepdims=True)
    return (x - m) / jnp.sqrt(v + eps)

def _scatter_add(tgt, idx, src, axis=0):
    return tgt.at[idx].add(src)

def _segment_sum(src, seg, n):
    return jax.ops.segment_sum(src, seg, n)
kernel_name = 'mk_dlrm_tower_d1_rec_r8_a99a77'

def setup_inputs(seed: int=0):
    np.random.seed(seed)
    _w = jnp.asarray

    def _rec_inputs():
        import jax
        import jax.numpy as jnp
        _tk = jax.random.key(seed)
        dense_ctx = jax.random.normal(jax.random.fold_in(_tk, 190), (2048, 16), jnp.float32)
        ids = jnp.stack([jax.random.randint(jax.random.fold_in(_tk, 200 + f), (2048,), 0, v, jnp.int32) for f, v in enumerate([125000, 1000, 1000, 1000, 12500, 1250, 12500, 1250, 1250, 1000, 1000, 125000, 12500, 125000, 12500, 1000, 1000, 12500, 12500, 12500, 1250, 12500, 1000, 1000, 1250, 1000, 1000, 1000, 1250, 1250, 1250, 1000])], axis=1)
        tbl_0 = 0.05 * jax.random.normal(jax.random.fold_in(_tk, 500 + 0), (125000, 64), jnp.float32)
        tbl_1 = 0.05 * jax.random.normal(jax.random.fold_in(_tk, 500 + 1), (1000, 64), jnp.float32)
        tbl_2 = 0.05 * jax.random.normal(jax.random.fold_in(_tk, 500 + 2), (1000, 64), jnp.float32)
        tbl_3 = 0.05 * jax.random.normal(jax.random.fold_in(_tk, 500 + 3), (1000, 64), jnp.float32)
        tbl_4 = 0.05 * jax.random.normal(jax.random.fold_in(_tk, 500 + 4), (12500, 64), jnp.float32)
        tbl_5 = 0.05 * jax.random.normal(jax.random.fold_in(_tk, 500 + 5), (1250, 64), jnp.float32)
        tbl_6 = 0.05 * jax.random.normal(jax.random.fold_in(_tk, 500 + 6), (12500, 64), jnp.float32)
        tbl_7 = 0.05 * jax.random.normal(jax.random.fold_in(_tk, 500 + 7), (1250, 64), jnp.float32)
        tbl_8 = 0.05 * jax.random.normal(jax.random.fold_in(_tk, 500 + 8), (1250, 64), jnp.float32)
        tbl_9 = 0.05 * jax.random.normal(jax.random.fold_in(_tk, 500 + 9), (1000, 64), jnp.float32)
        tbl_10 = 0.05 * jax.random.normal(jax.random.fold_in(_tk, 500 + 10), (1000, 64), jnp.float32)
        tbl_11 = 0.05 * jax.random.normal(jax.random.fold_in(_tk, 500 + 11), (125000, 64), jnp.float32)
        tbl_12 = 0.05 * jax.random.normal(jax.random.fold_in(_tk, 500 + 12), (12500, 64), jnp.float32)
        tbl_13 = 0.05 * jax.random.normal(jax.random.fold_in(_tk, 500 + 13), (125000, 64), jnp.float32)
        tbl_14 = 0.05 * jax.random.normal(jax.random.fold_in(_tk, 500 + 14), (12500, 64), jnp.float32)
        tbl_15 = 0.05 * jax.random.normal(jax.random.fold_in(_tk, 500 + 15), (1000, 64), jnp.float32)
        tbl_16 = 0.05 * jax.random.normal(jax.random.fold_in(_tk, 500 + 16), (1000, 64), jnp.float32)
        tbl_17 = 0.05 * jax.random.normal(jax.random.fold_in(_tk, 500 + 17), (12500, 64), jnp.float32)
        tbl_18 = 0.05 * jax.random.normal(jax.random.fold_in(_tk, 500 + 18), (12500, 64), jnp.float32)
        tbl_19 = 0.05 * jax.random.normal(jax.random.fold_in(_tk, 500 + 19), (12500, 64), jnp.float32)
        tbl_20 = 0.05 * jax.random.normal(jax.random.fold_in(_tk, 500 + 20), (1250, 64), jnp.float32)
        tbl_21 = 0.05 * jax.random.normal(jax.random.fold_in(_tk, 500 + 21), (12500, 64), jnp.float32)
        tbl_22 = 0.05 * jax.random.normal(jax.random.fold_in(_tk, 500 + 22), (1000, 64), jnp.float32)
        tbl_23 = 0.05 * jax.random.normal(jax.random.fold_in(_tk, 500 + 23), (1000, 64), jnp.float32)
        tbl_24 = 0.05 * jax.random.normal(jax.random.fold_in(_tk, 500 + 24), (1250, 64), jnp.float32)
        tbl_25 = 0.05 * jax.random.normal(jax.random.fold_in(_tk, 500 + 25), (1000, 64), jnp.float32)
        tbl_26 = 0.05 * jax.random.normal(jax.random.fold_in(_tk, 500 + 26), (1000, 64), jnp.float32)
        tbl_27 = 0.05 * jax.random.normal(jax.random.fold_in(_tk, 500 + 27), (1000, 64), jnp.float32)
        tbl_28 = 0.05 * jax.random.normal(jax.random.fold_in(_tk, 500 + 28), (1250, 64), jnp.float32)
        tbl_29 = 0.05 * jax.random.normal(jax.random.fold_in(_tk, 500 + 29), (1250, 64), jnp.float32)
        tbl_30 = 0.05 * jax.random.normal(jax.random.fold_in(_tk, 500 + 30), (1250, 64), jnp.float32)
        tbl_31 = 0.05 * jax.random.normal(jax.random.fold_in(_tk, 500 + 31), (1000, 64), jnp.float32)
        _rk = jax.random.fold_in(_tk, 7)
        W_top1 = 0.0441942 * jax.random.normal(jax.random.fold_in(_tk, 801), (512, 512), jnp.float32)
        W_top2 = 0.0441942 * jax.random.normal(jax.random.fold_in(_tk, 802), (512, 256), jnp.float32)
        W_top3 = 0.0625 * jax.random.normal(jax.random.fold_in(_tk, 803), (256, 1), jnp.float32)
        b_top1 = jnp.zeros((512,), jnp.float32)
        b_top2 = jnp.zeros((256,), jnp.float32)
        return (dense_ctx, ids, tbl_0, tbl_1, tbl_2, tbl_3, tbl_4, tbl_5, tbl_6, tbl_7, tbl_8, tbl_9, tbl_10, tbl_11, tbl_12, tbl_13, tbl_14, tbl_15, tbl_16, tbl_17, tbl_18, tbl_19, tbl_20, tbl_21, tbl_22, tbl_23, tbl_24, tbl_25, tbl_26, tbl_27, tbl_28, tbl_29, tbl_30, tbl_31, W_top1, b_top1, W_top2, b_top2, W_top3)
    dense_ctx, ids, tbl_0, tbl_1, tbl_2, tbl_3, tbl_4, tbl_5, tbl_6, tbl_7, tbl_8, tbl_9, tbl_10, tbl_11, tbl_12, tbl_13, tbl_14, tbl_15, tbl_16, tbl_17, tbl_18, tbl_19, tbl_20, tbl_21, tbl_22, tbl_23, tbl_24, tbl_25, tbl_26, tbl_27, tbl_28, tbl_29, tbl_30, tbl_31, W_top1, b_top1, W_top2, b_top2, W_top3 = _rec_inputs()

    def _L0_rec_setup():
        import jax, jax.numpy as jnp
        import numpy as np
        FIELDS = 32
        EMBED = 64
        BATCH = 1024
        PAIR = FIELDS * (FIELDS - 1) // 2

        def _pair_ids(fields):
            pairs = np.array([(i, j) for i in range(fields - 1) for j in range(i + 1, fields)], dtype=np.int32)
            return (jnp.asarray(pairs[:, 0]), jnp.asarray(pairs[:, 1]))
        key = jax.random.key(seed)
        k1, k2 = jax.random.split(key)
        inputs = jax.random.normal(k1, (BATCH, FIELDS, EMBED), dtype=jnp.float32)
        w = 0.05 * jax.random.normal(k2, (PAIR, EMBED, EMBED), dtype=jnp.float32)
        return {'inputs': inputs, 'w': w}
    _L0_rec_all = _L0_rec_setup()
    _L0_rec_in = {k: v for k, v in _L0_rec_all.items() if k in ('w',)}
    del _L0_rec_all
    return {'dense_ctx': dense_ctx, 'ids': ids, 'tbl_0': tbl_0, 'tbl_1': tbl_1, 'tbl_2': tbl_2, 'tbl_3': tbl_3, 'tbl_4': tbl_4, 'tbl_5': tbl_5, 'tbl_6': tbl_6, 'tbl_7': tbl_7, 'tbl_8': tbl_8, 'tbl_9': tbl_9, 'tbl_10': tbl_10, 'tbl_11': tbl_11, 'tbl_12': tbl_12, 'tbl_13': tbl_13, 'tbl_14': tbl_14, 'tbl_15': tbl_15, 'tbl_16': tbl_16, 'tbl_17': tbl_17, 'tbl_18': tbl_18, 'tbl_19': tbl_19, 'tbl_20': tbl_20, 'tbl_21': tbl_21, 'tbl_22': tbl_22, 'tbl_23': tbl_23, 'tbl_24': tbl_24, 'tbl_25': tbl_25, 'tbl_26': tbl_26, 'tbl_27': tbl_27, 'tbl_28': tbl_28, 'tbl_29': tbl_29, 'tbl_30': tbl_30, 'tbl_31': tbl_31, 'W_top1': W_top1, 'b_top1': b_top1, 'W_top2': W_top2, 'b_top2': b_top2, 'W_top3': W_top3, 'L0_rec_w': _L0_rec_in['w']}

def reference(dense_ctx, ids, tbl_0, tbl_1, tbl_2, tbl_3, tbl_4, tbl_5, tbl_6, tbl_7, tbl_8, tbl_9, tbl_10, tbl_11, tbl_12, tbl_13, tbl_14, tbl_15, tbl_16, tbl_17, tbl_18, tbl_19, tbl_20, tbl_21, tbl_22, tbl_23, tbl_24, tbl_25, tbl_26, tbl_27, tbl_28, tbl_29, tbl_30, tbl_31, W_top1, b_top1, W_top2, b_top2, W_top3, L0_rec_w):
    import jax
    import jax.numpy as jnp

    def _L0_rec_ref(inputs, w):
        import jax, jax.numpy as jnp
        import numpy as np
        FIELDS = 32
        EMBED = 64
        BATCH = 1024
        PAIR = FIELDS * (FIELDS - 1) // 2

        def _pair_ids(fields):
            pairs = np.array([(i, j) for i in range(fields - 1) for j in range(i + 1, fields)], dtype=np.int32)
            return (jnp.asarray(pairs[:, 0]), jnp.asarray(pairs[:, 1]))
        ids_x, ids_y = _pair_ids(FIELDS)
        p = inputs[:, ids_x, :]
        q = inputs[:, ids_y, :]
        pw = jnp.einsum('bpi,pij->bpj', p, w)
        out = jnp.einsum('bpj,bpj->bp', pw, q)
        return out
    e = jnp.stack([tbl_0[ids[:, 0]], tbl_1[ids[:, 1]], tbl_2[ids[:, 2]], tbl_3[ids[:, 3]], tbl_4[ids[:, 4]], tbl_5[ids[:, 5]], tbl_6[ids[:, 6]], tbl_7[ids[:, 7]], tbl_8[ids[:, 8]], tbl_9[ids[:, 9]], tbl_10[ids[:, 10]], tbl_11[ids[:, 11]], tbl_12[ids[:, 12]], tbl_13[ids[:, 13]], tbl_14[ids[:, 14]], tbl_15[ids[:, 15]], tbl_16[ids[:, 16]], tbl_17[ids[:, 17]], tbl_18[ids[:, 18]], tbl_19[ids[:, 19]], tbl_20[ids[:, 20]], tbl_21[ids[:, 21]], tbl_22[ids[:, 22]], tbl_23[ids[:, 23]], tbl_24[ids[:, 24]], tbl_25[ids[:, 25]], tbl_26[ids[:, 26]], tbl_27[ids[:, 27]], tbl_28[ids[:, 28]], tbl_29[ids[:, 29]], tbl_30[ids[:, 30]], tbl_31[ids[:, 31]]], axis=1)
    z = _L0_rec_ref(e, L0_rec_w)
    z = z.reshape(z.shape[0], -1)
    h = jnp.concatenate([z, dense_ctx], axis=1)
    h = jnp.maximum(h @ W_top1 + b_top1, 0.0)
    h = jnp.maximum(h @ W_top2 + b_top2, 0.0)
    y = h @ W_top3
    return y

_drawn_inputs = setup_inputs


def setup_inputs(seed=0):
    import zlib

    import numpy as np

    out = dict(_drawn_inputs(seed))
    spreads = {'b_top1': (0.0, 0.1), 'b_top2': (0.0, 0.1)}
    factors = {'tbl_0': 6.305,
     'tbl_1': 5.962,
     'tbl_2': 5.844,
     'tbl_3': 5.538,
     'tbl_4': 4.872,
     'tbl_5': 6.279,
     'tbl_6': 5.496,
     'tbl_7': 4.922,
     'tbl_8': 5.735,
     'tbl_9': 5.592,
     'tbl_10': 5.69,
     'tbl_11': 5.374,
     'tbl_12': 5.344,
     'tbl_13': 5.157,
     'tbl_14': 5.902,
     'tbl_15': 5.59,
     'tbl_16': 5.172,
     'tbl_17': 5.959,
     'tbl_18': 5.068,
     'tbl_19': 5.357,
     'tbl_20': 5.117,
     'tbl_21': 5.738,
     'tbl_22': 5.961,
     'tbl_23': 5.823,
     'tbl_24': 5.973,
     'tbl_25': 5.197,
     'tbl_26': 5.745,
     'tbl_27': 5.66,
     'tbl_28': 5.843,
     'tbl_29': 5.661,
     'tbl_30': 5.509,
     'tbl_31': 6.114}
    for name, (base, spread) in spreads.items():
        noise = np.random.default_rng([zlib.crc32(name.encode()), seed]).standard_normal(out[name].shape)
        drawn = base * np.exp(spread * noise) if base else spread * noise
        out[name] = jnp.asarray(drawn.astype(out[name].dtype))
    for name, factor in factors.items():
        out[name] = (out[name] * factor).astype(out[name].dtype)
    return out
```

```python
from contextlib import ExitStack

import concourse.bass as bass
from concourse import mybir

BATCH, FIELDS, EMBED, CTX = 2048, 32, 64, 16
HID1, HID2 = 512, 256
P = 128
TILE = 512
TILES = BATCH // TILE
SUBS = TILE // P
DUOS = FIELDS // 2
PAIRS = FIELDS * (FIELDS - 1) // 2


def pair_index(i, j):
    return i * (FIELDS - 1) - i * (i - 1) // 2 + j - i - 1


def order_chunks():
    chunks, ops = [], []
    for i in range(FIELDS - 2, -1, -1):
        low, top = (i + 2) // 2 if i % 2 == 0 else (i + 1) // 2, DUOS - 1
        half = i % 2 == 0
        while top >= low or half:
            c = len(chunks)
            if half and (c % 4 == 3 or top < low):
                chunks.append((i, i // 2, True))
                ops.append((c, 1))
                half = False
            elif top == low or c % 4 == 3:
                chunks.append((i, top, False))
                ops.append((c, 1))
                top -= 1
            else:
                chunks += [(i, top - 1, False), (i, top, False)]
                ops.append((c, 2))
                top -= 2
    return chunks, ops


CHUNKS, OPS = order_chunks()
NCHUNK = len(CHUNKS)
ROUND = 4
ROUNDS = NCHUNK // ROUND
KTILES = NCHUNK * 2 // P
ROUNDS_KT = ROUNDS // KTILES
HALVES = [c for c, (_, _, half) in enumerate(CHUNKS) if half]
LAST_OF_STEP = {i: max(c for c, ch in enumerate(CHUNKS) if ch[0] == i) for i in range(FIELDS - 1)}
FIRST_OF_STEP = {i: min(c for c, ch in enumerate(CHUNKS) if ch[0] == i) for i in range(FIELDS - 1)}
OPS_THROUGH = {}
for _n, (_c, _k) in enumerate(OPS):
    for _d in range(_k):
        OPS_THROUGH[_c + _d] = _n + 1
NOPS = len(OPS)


SLOT_PAIRS = 31


def order_groups():
    groups, cur = [], []
    for i in range(FIELDS - 2, -1, -1):
        if cur and sum(FIELDS - 1 - k for k in cur) + FIELDS - 1 - i > SLOT_PAIRS:
            groups.append(cur)
            cur = []
        cur.append(i)
    return groups + [cur]


GROUPS = order_groups()
NGROUP = len(GROUPS)
GROUP_OF = {i: g for g, steps in enumerate(GROUPS) for i in steps}
G_FIRST = [pair_index(steps[-1], steps[-1] + 1) for steps in GROUPS]
G_PAIRS = [sum(FIELDS - 1 - i for i in steps) for steps in GROUPS]
WSLOTS = 4
assert NGROUP % WSLOTS == 0
MSLOTS = 4
MLP_STEPS = HID1 // P + HID2 // P + 1
GATHERS = 16 * 2 * SUBS


def z_row(c, upper):
    r, g = divmod(c, ROUND)
    kt, s = divmod(r, ROUNDS_KT)
    return kt * P + 32 * g + 2 * s + upper


def w1_rows():
    rows = [0] * (KTILES * P)
    for c, (i, q, half) in enumerate(CHUNKS):
        rows[z_row(c, 0)] = PAIRS + HALVES.index(c) if half else pair_index(i, 2 * q)
        rows[z_row(c, 1)] = pair_index(i, 2 * q + 1)
    return rows


def order_events(first):
    ev = []
    if first:
        ev += [("weights", 0), ("duo", 15), ("split", 15), ("weights", 1), ("duo", 14), ("split", 14),
               ("weights", 2), ("duo", 13), ("split", 13), ("duo", 12)]
        tail = []
    else:
        ev += [("duo", 15), ("reduce", -1), ("zout", -1), ("split", 15), ("duo", 14), ("split", 14),
               ("mlp", 0), ("duo", 13), ("split", 13), ("mlp", 1), ("duo", 12), ("mlp", 2)]
        tail = [("mlp", n) for n in range(3, MLP_STEPS)]
    late = [("split", 12)]
    for r in range(ROUNDS):
        ev.append(("round", r))
        if r:
            ev.append(("reduce", r - 1))
            if r % ROUNDS_KT == 0:
                ev.append(("zout", r // ROUNDS_KT - 1))
        ev += late
        late = []
        if tail:
            ev.append(tail.pop(0))
        for m in range(DUOS - MSLOTS - 1, -1, -1):
            if LAST_OF_STEP[2 * (m + MSLOTS)] // ROUND == r:
                ev.append(("duo", m)) if not late else ev.extend(late + [("duo", m)])
                late = [("split", m)]
        if first:
            for g in range(3, NGROUP):
                if (LAST_OF_STEP[GROUPS[g - WSLOTS][-1]] // ROUND if g >= WSLOTS else 0) == r:
                    ev.append(("weights", g))
    return ev + late


def dlrm_tower(nc, const, ids, wsrc, w1, w2, w3, b1, b2, ctx_t, tables, out):
    F32, F32R, I32 = mybir.dt.float32, mybir.dt.float32r, mybir.dt.int32
    ALU, ACT = mybir.AluOpType, mybir.ActivationFunctionType
    SLOT = SLOT_PAIRS * EMBED
    LOW, UP = slice(0, EMBED), slice(EMBED, P)

    with ExitStack() as stack:
        def sb(name, shape, dt=F32):
            return stack.enter_context(nc.sbuf_tensor(name, shape, dt))

        def sem(name):
            return stack.enter_context(nc.semaphore(name))

        const_sb = sb("const_sb", [P, const.shape[1]])
        ident = const_sb[:, 0:P]
        sel = const_sb[:, P:P + 62]
        half_sel = const_sb[:, P + 62:].rearrange("p (h n) -> p h n", n=32)
        idx = sb("idx", [P, FIELDS * SUBS], I32)
        emb = sb("emb", [P, DUOS, SUBS, P])
        e_t = sb("e_t", [P, DUOS, TILE])
        halves = sb("halves", [P, MSLOTS, 2, 2, TILE], F32R)
        w_sb = sb("w_sb", [P, WSLOTS, EMBED + SLOT], F32R)
        shared = sb("shared", [P, 2 * SLOT])
        raw_w = shared[:, :].rearrange("p (s n) -> p s n", s=2)
        h1 = shared[:, 0:HID1 // P * TILE].rearrange("p (m n) -> p m n", n=TILE)
        h2 = sb("h2", [P, HID2 // P, TILE])
        prod = sb("prod", [P, 2 * ROUND, TILE])
        half_prod = sb("half_prod", [P, 2, TILE])
        z_sb = sb("z_sb", [P, KTILES, TILE])
        w1_sb = sb("w1_sb", [P, KTILES, HID1])
        w2_sb = sb("w2_sb", [P, HID1 // P, HID2])
        w3_sb = sb("w3_sb", [P, HID2 // P])
        b1_sb = sb("b1_sb", [P, HID1 // P])
        b2_sb = sb("b2_sb", [P, HID2 // P])
        y_sb = sb("y_sb", [1, TILE])
        w_split = nc.dram_tensor("w_split", [P, PAIRS * EMBED], F32)

        main_ps = stack.enter_context(nc.psum_tensor("main_ps", [P, ROUND, TILE], F32))
        z_ps = stack.enter_context(nc.psum_tensor("z_ps", [P, 2, TILE], F32))
        t_ps = stack.enter_context(nc.psum_tensor("t_ps", [P, TILE], F32))
        y_ps = stack.enter_context(nc.psum_tensor("y_ps", [P, TILE], F32))

        const_in = sem("const_in")
        mlp_in = sem("mlp_in")
        ctx_in = sem("ctx_in")
        idx_in = sem("idx_in")
        gathered = [sem(f"gathered{m}") for m in range(DUOS)]
        raw_in = [sem(f"raw_in{s}") for s in range(2)]
        stored = [sem(f"stored{s}") for s in range(WSLOTS)]
        w_in = [sem(f"w_in{s}") for s in range(WSLOTS)]
        w_hi = sem("w_hi")
        w_ready = sem("w_ready")
        cleared = sem("cleared")
        transposed = sem("transposed")
        e_hi = sem("e_hi")
        e_kept = sem("e_kept")
        e_lo = sem("e_lo")
        moving = sem("moving")
        mains = sem("mains")
        products = sem("products")
        reduced = sem("reduced")
        z_out = sem("z_out")
        mlp_ps = sem("mlp_ps")
        mlp_act = sem("mlp_act")
        y_out = sem("y_out")
        block = stack.enter_context(nc.Block())

        def duo_done(t, m):
            return DUOS * t + DUOS - m

        def w_columns(c):
            i, q, half = CHUNKS[c]
            g = GROUP_OF[i]
            p = pair_index(i, 2 * q + 1) - 1 - G_FIRST[g]
            return w_sb[:, g % WSLOTS, (p + 1) * EMBED:(p + 3) * EMBED]

        @block.gpsimd
        def _(pool):
            def tile(t, first):
                pool.dma_start(idx[:, :], ids[bass.ds(t, 1)].rearrange("a p n -> (a p) n")).then_inc(idx_in, 16)
                pool.wait_ge(idx_in, 16 * t + 16)
                pool.nop(nofuse=True)
                for m in range(DUOS - 1, -1, -1):
                    if not first:
                        pool.wait_ge(transposed, duo_done(t - 1, m))
                        pool.nop(nofuse=True)
                    for odd in (1, 0):
                        f = 2 * m + odd
                        for s in range(SUBS):
                            pool.indirect_dma_start(
                                out=emb[:, m, s, odd * EMBED:(odd + 1) * EMBED], out_offset=None, in_=tables[f],
                                in_offset=bass.IndirectOffsetOnAxis(ap=idx[:, f * SUBS + s:f * SUBS + s + 1], axis=0),
                            ).then_inc(gathered[m], 16)
                for m in range(DUOS):
                    pool.wait_ge(gathered[m], GATHERS * (t + 1))

            tile(0, True)
            with pool.Fori(1, TILES) as t:
                tile(t, False)

        @block.sync
        def _(sp):
            def load_raw(g):
                if g >= 2:
                    sp.wait_ge(w_ready, g - 1)
                src = wsrc[:, G_FIRST[g] * EMBED:(G_FIRST[g] + G_PAIRS[g]) * EMBED]
                for rows in (LOW, UP):
                    sp.dma_start(raw_w[rows, g % 2, 0:G_PAIRS[g] * EMBED], src).then_inc(raw_in[g % 2], 16)

            def store_split(g):
                sp.wait_ge(w_ready, g + 1)
                cols = slice(G_FIRST[g] * EMBED, (G_FIRST[g] + G_PAIRS[g]) * EMBED)
                sp.dma_start(w_split[:, cols], w_sb[:, g % WSLOTS, EMBED:EMBED + G_PAIRS[g] * EMBED].bitcast(F32))\
                  .then_inc(stored[g % WSLOTS], 16)

            def load_ctx(t, first):
                if not first:
                    sp.wait_ge(reduced, ROUNDS * (t - 1) + HALVES[-1] // ROUND + 1)
                for n in range(2):
                    sp.dma_start(half_prod[0:CTX, n, :], ctx_t[:, bass.ds(t * TILE, TILE)]).then_inc(ctx_in, 16)

            sp.sem_inc(y_out, 16)
            load_raw(0)
            sp.dma_start(const_sb[:, :], const).then_inc(const_in, 16)
            load_raw(1)
            sp.wait_ge(cleared, 1)
            load_ctx(0, True)
            for g in range(NGROUP):
                store_split(g)
                if g + 2 < NGROUP:
                    load_raw(g + 2)
                if g == 2:
                    for dst, src in ((w1_sb, w1), (w2_sb, w2)):
                        sp.dma_start(dst[:, :, :], src).then_inc(mlp_in, 16)
                    for dst, src in ((w3_sb, w3), (b1_sb, b1), (b2_sb, b2)):
                        sp.dma_start(dst[:, :], src).then_inc(mlp_in, 16)
            for s in range(WSLOTS):
                sp.wait_ge(stored[s], 16 * (NGROUP // WSLOTS))

            def load_split(t, g):
                prev_t, prev_g = (t, g - WSLOTS) if g >= WSLOTS else (t - 1, g - WSLOTS + NGROUP)
                sp.wait_ge(mains, NCHUNK * prev_t + LAST_OF_STEP[GROUPS[prev_g][-1]] + 1)
                cols = slice(G_FIRST[g] * EMBED, (G_FIRST[g] + G_PAIRS[g]) * EMBED)
                sp.dma_start(w_sb[:, g % WSLOTS, EMBED:EMBED + G_PAIRS[g] * EMBED].bitcast(F32), w_split[:, cols])\
                  .then_inc(w_in[g % WSLOTS], 16)

            def store_y(t):
                sp.wait_ge(mlp_act, MLP_STEPS * (t + 1) + 1)
                sp.dma_start(out[:, bass.ds(t * TILE, TILE)], y_sb[:, :]).then_inc(y_out, 16)

            with sp.Fori(1, TILES) as t:
                for g in range(NGROUP):
                    load_split(t, g)
                    if g == WSLOTS - 2:
                        load_ctx(t, False)
                    if g == WSLOTS + 1:
                        store_y(t - 1)
            store_y(TILES - 1)
            sp.wait_ge(y_out, 16 * (TILES + 1))

        @block.tensor
        def _(pe):
            def transpose_duo(t, m):
                pe.wait_ge(gathered[m], GATHERS * (t + 1))
                for s in range(SUBS):
                    last = nc.tensor.transpose(t_ps[:, s * P:(s + 1) * P], emb[:, m, s, :], ident)
                last.then_inc(transposed, 1)

            def main_products(t, r, first):
                for c in range(ROUND * r, ROUND * r + ROUND):
                    i, q, half = CHUNKS[c]
                    if c == FIRST_OF_STEP[i]:
                        pe.wait_ge(moving, FIELDS * t + FIELDS - i)
                        g = GROUP_OF[i]
                        if i == GROUPS[g][0]:
                            if first:
                                pe.wait_ge(w_ready, g + 1)
                            else:
                                pe.wait_ge(w_in[g % WSLOTS], 16 * ((t - 1) * (NGROUP // WSLOTS) + g // WSLOTS + 1))
                    if c >= ROUND:
                        pe.wait_ge(products, NOPS * t + OPS_THROUGH[c - ROUND])
                    elif not first:
                        pe.wait_ge(products, NOPS * (t - 1) + OPS_THROUGH[c - ROUND + NCHUNK])
                    m, odd = divmod(i, 2)
                    nc.tensor.matmul(main_ps[:, c % ROUND, :], w_columns(c), halves[:, m % MSLOTS, odd, 0, :],
                                     start=True, stop=False)
                    nc.tensor.matmul(main_ps[:, c % ROUND, :], w_columns(c), halves[:, m % MSLOTS, odd, 1, :],
                                     start=False, stop=True).then_inc(mains, 1)

            def reduce_round(t, r):
                kt, s = divmod(r, ROUNDS_KT)
                if s == 0 and not (isinstance(t, int) and KTILES * t + kt < 2):
                    pe.wait_ge(z_out, KTILES * t + kt - 1)
                pe.wait_ge(products, NOPS * t + OPS_THROUGH[ROUND * r + ROUND - 1])
                for g in range(ROUND):
                    c = ROUND * r + g
                    if CHUNKS[c][2]:
                        h = HALVES.index(c)
                        if h < 2:
                            pe.wait_ge(ctx_in, 32 * (t + 1))
                        which, what = half_sel[:, h, :], half_prod[:, h % 2, :]
                    else:
                        which, what = sel[:, 30 - 2 * s:62 - 2 * s], prod[:, c % (2 * ROUND), :]
                    last = nc.tensor.matmul(z_ps[32 * g:32 * g + 32, kt % 2, :], which, what,
                                            start=(s == 0), stop=(s == ROUNDS_KT - 1))
                last.then_inc(reduced, 1)

            def mlp(t, n):
                if n == 0:
                    pe.wait_ge(z_out, KTILES * (t + 1))
                pe.wait_ge(mlp_act, MLP_STEPS * t + n + 1)
                if n < HID1 // P:
                    w, x, m = w1_sb, z_sb, n
                elif n < MLP_STEPS - 1:
                    w, x, m = w2_sb, h1, n - HID1 // P
                else:
                    for k in range(HID2 // P):
                        last = nc.tensor.matmul(y_ps[0:1, :], w3_sb[:, k:k + 1], h2[:, k, :],
                                                start=(k == 0), stop=(k == HID2 // P - 1))
                    last.then_inc(mlp_ps, 1)
                    return
                for k in range(KTILES):
                    last = nc.tensor.matmul(y_ps[:, :], w[:, k, m * P:(m + 1) * P], x[:, k, :],
                                            start=(k == 0), stop=(k == KTILES - 1))
                last.then_inc(mlp_ps, 1)

            def tile(t, first):
                for kind, n in order_events(first):
                    if kind == "duo":
                        if not (first and n == DUOS - 1):
                            pe.wait_ge(e_lo, duo_done(t, n) - 1)
                        transpose_duo(t, n)
                    elif kind == "round":
                        main_products(t, n, first)
                    elif kind == "reduce":
                        reduce_round(t, n) if n >= 0 else reduce_round(t - 1, ROUNDS - 1)
                    elif kind == "mlp":
                        mlp(t - 1, n)

            pe.wait_ge(const_in, 16)
            pe.wait_ge(cleared, 2)
            tile(0, True)
            pe.wait_ge(mlp_in, 5 * 16)
            with pe.Fori(1, TILES) as t:
                tile(t, False)
            reduce_round(TILES - 1, ROUNDS - 1)
            for n in range(MLP_STEPS):
                mlp(TILES - 1, n)

        @block.vector
        def _(dve):
            nc.vector.memset(half_prod[LOW, :, :], 0.0).then_inc(cleared, 1)
            nc.vector.memset(w_sb[:, :, 0:EMBED].bitcast(F32), 0.0).then_inc(cleared, 1)

            def low_weights(g):
                dve.wait_ge(w_hi, g + 1)
                n = G_PAIRS[g] * EMBED
                dst = w_sb[UP, g % WSLOTS, EMBED:EMBED + n]
                nc.vector.tensor_tensor(dst, raw_w[UP, g % 2, 0:n], dst.bitcast(F32), ALU.subtract).then_inc(w_ready, 1)

            def low_duo(t, m):
                dve.wait_ge(e_hi, duo_done(t, m))
                dve.wait_ge(e_kept, duo_done(t, m))
                nc.vector.tensor_tensor(halves[:, m % MSLOTS, 0, 1, :], t_ps[:, :],
                                        halves[:, m % MSLOTS, 0, 0, :].bitcast(F32), ALU.subtract).then_inc(e_lo, 1)

            def multiply(t, r, first):
                for c, k in OPS:
                    if c // ROUND != r:
                        continue
                    i, q, half = CHUNKS[c]
                    dve.wait_ge(mains, NCHUNK * t + c + k)
                    if half:
                        before = HALVES.index(c) - 2
                        if before >= 0:
                            dve.wait_ge(reduced, ROUNDS * t + HALVES[before] // ROUND + 1)
                        elif not first:
                            dve.wait_ge(reduced, ROUNDS * (t - 1) + HALVES[before] // ROUND + 1)
                        nc.vector.tensor_tensor(half_prod[UP, HALVES.index(c) % 2, :], main_ps[UP, c % ROUND, :],
                                                e_t[UP, q, :], ALU.mult).then_inc(products, 1)
                        continue
                    if r >= 2 or not first:
                        dve.wait_ge(reduced, ROUNDS * t + r - 1)
                    a, s = c % ROUND, c % (2 * ROUND)
                    nc.vector.tensor_tensor(prod[:, s:s + k, :], main_ps[:, a:a + k, :], e_t[:, q:q + k, :],
                                            ALU.mult).then_inc(products, 1)

            def tile(t, first):
                for kind, n in order_events(first):
                    if kind == "weights":
                        low_weights(n)
                    elif kind == "split":
                        low_duo(t, n)
                    elif kind == "round":
                        multiply(t, n, first)

            tile(0, True)
            with dve.Fori(1, TILES) as t:
                tile(t, False)

        @block.scalar
        def _(act):
            def copy(dst, src):
                return nc.scalar.activation(dst, src, ACT.Copy)

            def high_weights(g):
                act.wait_ge(raw_in[g % 2], 32 * (g // 2 + 1))
                if g >= WSLOTS:
                    act.wait_ge(mains, LAST_OF_STEP[GROUPS[g - WSLOTS][-1]] + 1)
                    act.wait_ge(stored[g % WSLOTS], 16 * (g // WSLOTS))
                n = G_PAIRS[g] * EMBED
                copy(w_sb[:, g % WSLOTS, EMBED:EMBED + n], raw_w[:, g % 2, 0:n]).then_inc(w_hi, 1)

            def high_duo(t, m, first):
                act.wait_ge(transposed, duo_done(t, m))
                if m + MSLOTS < DUOS:
                    act.wait_ge(mains, NCHUNK * t + LAST_OF_STEP[2 * (m + MSLOTS)] + 1)
                elif not first:
                    act.wait_ge(mains, NCHUNK * (t - 1) + LAST_OF_STEP[2 * (m + MSLOTS - DUOS)] + 1)
                copy(halves[:, m % MSLOTS, 0, 0, :], t_ps[:, :]).then_inc(e_hi, 1)
                if not first:
                    last = max(c for c, ch in enumerate(CHUNKS) if ch[1] == m)
                    act.wait_ge(products, NOPS * (t - 1) + OPS_THROUGH[last])
                copy(e_t[:, m, :], t_ps[:, :]).then_inc(e_kept, 1)

            def spread_duo(t, m):
                act.wait_ge(e_lo, duo_done(t, m))
                even, odd = halves[:, m % MSLOTS, 0], halves[:, m % MSLOTS, 1]
                for rows in (LOW, UP):
                    for n in range(2):
                        last = copy(odd[rows, n, :], even[UP, n, :].bitcast(F32))
                last.then_inc(moving, 1)
                act.wait_ge(moving, FIELDS * t + FIELDS - 1 - 2 * m)
                for n in range(2):
                    last = copy(even[UP, n, :], even[LOW, n, :].bitcast(F32))
                last.then_inc(moving, 1)

            def z_tile(t, kt):
                act.wait_ge(reduced, ROUNDS * t + ROUNDS_KT * (kt + 1))
                if kt == 0 and not (isinstance(t, int) and t == 0):
                    act.wait_ge(mlp_ps, MLP_STEPS * (t - 1) + HID1 // P)
                copy(z_sb[:, kt, :], z_ps[:, kt % 2, :]).then_inc(z_out, 1)

            def mlp(t, n):
                act.wait_ge(mlp_ps, MLP_STEPS * t + n + 1)
                if n < HID1 // P:
                    ins = nc.scalar.activation(h1[:, n, :], y_ps[:, :], ACT.Relu, bias=b1_sb[:, n:n + 1])
                elif n < MLP_STEPS - 1:
                    m = n - HID1 // P
                    ins = nc.scalar.activation(h2[:, m, :], y_ps[:, :], ACT.Relu, bias=b2_sb[:, m:m + 1])
                else:
                    act.wait_ge(y_out, 16 * (t + 1))
                    ins = copy(y_sb[:, :], y_ps[0:1, :])
                ins.then_inc(mlp_act, 1)

            def tile(t, first):
                for kind, n in order_events(first):
                    if kind == "weights":
                        high_weights(n)
                    elif kind == "duo":
                        high_duo(t, n, first)
                    elif kind == "split":
                        spread_duo(t, n)
                    elif kind == "zout":
                        z_tile(t, n) if n >= 0 else z_tile(t - 1, KTILES - 1)
                    elif kind == "mlp":
                        mlp(t - 1, n)

            act.sem_inc(mlp_act, 1)
            tile(0, True)
            act.wait_ge(mlp_in, 5 * 16)
            with act.Fori(1, TILES) as t:
                tile(t, False)
            z_tile(TILES - 1, KTILES - 1)
            for n in range(MLP_STEPS):
                mlp(TILES - 1, n)


def kernel(**inputs):
    import numpy as np
    import concourse.bacc as bacc
    from concourse.bass_utils import run_bass_kernel_spmd

    nc = bacc.Bacc("TRN2", target_bir_lowering=False, num_devices=1)

    const = np.zeros((P, P + 62 + 32 * CTX), np.float32)
    const[:, :P] = np.eye(P, dtype=np.float32)
    const[:EMBED, P + 30] = 1
    const[EMBED:, P + 31] = 1
    for h, c in enumerate(HALVES):
        s = c // ROUND % ROUNDS_KT
        const[h, P + 62 + 32 * h + 2 * s] = 1
        const[EMBED:, P + 62 + 32 * h + 2 * s + 1] = 1

    a = {k: np.asarray(v) for k, v in inputs.items()}
    arrays = {
        "const": const,
        "ids": a["ids"].reshape(TILES, SUBS, P, FIELDS).transpose(0, 2, 3, 1).reshape(TILES, P, FIELDS * SUBS),
        "w": a["L0_rec_w"].transpose(1, 0, 2).reshape(EMBED, PAIRS * EMBED),
        "w1": a["W_top1"][w1_rows()].reshape(KTILES, P, HID1).transpose(1, 0, 2),
        "w2": a["W_top2"].reshape(HID1 // P, P, HID2).transpose(1, 0, 2),
        "w3": a["W_top3"].reshape(HID2 // P, P).T,
        "b1": a["b_top1"].reshape(HID1 // P, P).T,
        "b2": a["b_top2"].reshape(HID2 // P, P).T,
        "ctx": a["dense_ctx"].T,
    }
    for f in range(FIELDS):
        arrays[f"tbl_{f}"] = a[f"tbl_{f}"]
    arrays = {f"in_{k}": np.ascontiguousarray(v) for k, v in arrays.items()}
    ap = {k: nc.dram_tensor(k, v.shape, mybir.dt.from_np(v.dtype), kind="ExternalInput").ap()
          for k, v in arrays.items()}
    out = nc.dram_tensor("out_y", (1, BATCH), mybir.dt.float32, kind="ExternalOutput").ap()
    dlrm_tower(nc, ap["in_const"], ap["in_ids"], ap["in_w"], ap["in_w1"], ap["in_w2"], ap["in_w3"], ap["in_b1"],
               ap["in_b2"], ap["in_ctx"], [ap[f"in_tbl_{f}"] for f in range(FIELDS)], out)
    r = run_bass_kernel_spmd(nc, [arrays], core_ids=[0])
    return r.results[0]["out_y"].reshape(BATCH, 1)
```

```python
from contextlib import ExitStack

import concourse.bass as bass
from concourse import mybir

BATCH, FIELDS, EMBED, CTX = 2048, 32, 64, 16
HID1, HID2 = 512, 256
P = 128
TILE = 512
TILES = BATCH // TILE
SUBS = TILE // P
DUOS = FIELDS // 2
PAIRS = FIELDS * (FIELDS - 1) // 2


def pair_index(i, j):
    return i * (FIELDS - 1) - i * (i - 1) // 2 + j - i - 1


def order_chunks():
    chunks, ops = [], []
    for i in range(FIELDS - 2, -1, -1):
        low, top = (i + 2) // 2 if i % 2 == 0 else (i + 1) // 2, DUOS - 1
        half = i % 2 == 0
        while top >= low or half:
            c = len(chunks)
            if half and (c % 4 == 3 or top < low):
                chunks.append((i, i // 2, True))
                ops.append((c, 1))
                half = False
            elif top == low or c % 4 == 3:
                chunks.append((i, top, False))
                ops.append((c, 1))
                top -= 1
            else:
                chunks += [(i, top - 1, False), (i, top, False)]
                ops.append((c, 2))
                top -= 2
    return chunks, ops


CHUNKS, OPS = order_chunks()
NCHUNK = len(CHUNKS)
ROUND = 4
ROUNDS = NCHUNK // ROUND
KTILES = NCHUNK * 2 // P
ROUNDS_KT = ROUNDS // KTILES
HALVES = [c for c, (_, _, half) in enumerate(CHUNKS) if half]
LAST_OF_STEP = {i: max(c for c, ch in enumerate(CHUNKS) if ch[0] == i) for i in range(FIELDS - 1)}
FIRST_OF_STEP = {i: min(c for c, ch in enumerate(CHUNKS) if ch[0] == i) for i in range(FIELDS - 1)}
OPS_THROUGH = {}
for _n, (_c, _k) in enumerate(OPS):
    for _d in range(_k):
        OPS_THROUGH[_c + _d] = _n + 1
NOPS = len(OPS)


SLOT_PAIRS = 31


def order_groups():
    groups, cur = [], []
    for i in range(FIELDS - 2, -1, -1):
        if cur and sum(FIELDS - 1 - k for k in cur) + FIELDS - 1 - i > SLOT_PAIRS:
            groups.append(cur)
            cur = []
        cur.append(i)
    return groups + [cur]


GROUPS = order_groups()
NGROUP = len(GROUPS)
GROUP_OF = {i: g for g, steps in enumerate(GROUPS) for i in steps}
G_FIRST = [pair_index(steps[-1], steps[-1] + 1) for steps in GROUPS]
G_PAIRS = [sum(FIELDS - 1 - i for i in steps) for steps in GROUPS]
WSLOTS = 4
assert NGROUP % WSLOTS == 0
MSLOTS = 4
MLP_STEPS = HID1 // P + HID2 // P + 1
GATHERS = 16 * 2 * SUBS


def z_row(c, upper):
    r, g = divmod(c, ROUND)
    kt, s = divmod(r, ROUNDS_KT)
    return kt * P + 32 * g + 2 * s + upper


def w1_rows():
    rows = [0] * (KTILES * P)
    for c, (i, q, half) in enumerate(CHUNKS):
        rows[z_row(c, 0)] = PAIRS + HALVES.index(c) if half else pair_index(i, 2 * q)
        rows[z_row(c, 1)] = pair_index(i, 2 * q + 1)
    return rows


FIRST_OF_DUO = {m: FIRST_OF_STEP[min(2 * m + 1, FIELDS - 2)] for m in range(DUOS)}
MLP_AFTER_ROUND = {0: 2, 1: 2, 2: 1, 3: 1, 4: 1}
AHEAD = 3


def order_events(first, last):
    ev, duos, weights, blocks = [], [], [], []
    if first:
        for n in range(AHEAD):
            ev += [("whigh", n), ("wlow", n), ("duo", DUOS - 1 - n), ("split", DUOS - 1 - n)]
    else:
        blocks = [("mlp", n) for n in range(MLP_STEPS)]
    for m in range(DUOS - 1 - AHEAD, -1, -1):
        free = LAST_OF_STEP[2 * (m + MSLOTS)] // ROUND if m + MSLOTS < DUOS else -1
        soon = FIRST_OF_DUO[m] // ROUND - (3 if first else 5)
        duos.append((max(free, soon), m))
    if not last:
        for m in range(DUOS - 1, DUOS - 1 - AHEAD, -1):
            duos.append((next(c for c, ch in enumerate(CHUNKS) if ch[:2] == (0, m)) // ROUND, m - DUOS))
    if first:
        for g in range(AHEAD, NGROUP):
            free = LAST_OF_STEP[GROUPS[g - WSLOTS][-1]] // ROUND if g >= WSLOTS else -1
            weights.append((max(free, FIRST_OF_STEP[GROUPS[g][0]] // ROUND - 4), g))
    split, low = [], []
    for r in range(-1, ROUNDS):
        if r >= 0:
            ev.append(("round", r))
            if r or not first:
                ev.append(("reduce", r - 1))
            if r % ROUNDS_KT == 0 and (r or not first):
                ev.append(("zout", r // ROUNDS_KT - 1))
            ev += split + low
            split, low = [], []
            for _ in range(MLP_AFTER_ROUND.get(r, 0) if blocks else 0):
                ev.append(blocks.pop(0))
        if duos and duos[0][0] <= r and not split:
            m = duos.pop(0)[1]
            ev.append(("duo", m))
            split = [("split", m)]
        if weights and weights[0][0] <= r:
            g = weights.pop(0)[1]
            ev.append(("whigh", g))
            low = [("wlow", g)]
    return ev + split + low + [("duo", m) if k == 0 else ("split", m) for _, m in duos for k in (0, 1)]


def dlrm_tower(nc, const, ids, wsrc, w1, w2, w3, b1, b2, ctx_t, tables, out):
    F32, F32R, I32 = mybir.dt.float32, mybir.dt.float32r, mybir.dt.int32
    ALU, ACT = mybir.AluOpType, mybir.ActivationFunctionType
    SLOT = SLOT_PAIRS * EMBED
    LOW, UP = slice(0, EMBED), slice(EMBED, P)

    with ExitStack() as stack:
        def sb(name, shape, dt=F32):
            return stack.enter_context(nc.sbuf_tensor(name, shape, dt))

        def sem(name):
            return stack.enter_context(nc.semaphore(name))

        const_sb = sb("const_sb", [P, const.shape[1]])
        ident = const_sb[:, 0:P]
        sel = const_sb[:, P:P + 62]
        half_sel = const_sb[:, P + 62:].rearrange("p (h n) -> p h n", n=32)
        idx = sb("idx", [P, FIELDS * SUBS], I32)
        emb = sb("emb", [P, DUOS, SUBS, P])
        e_t = sb("e_t", [P, DUOS, TILE])
        halves = sb("halves", [P, MSLOTS, 2, 2, TILE], F32R)
        w_sb = sb("w_sb", [P, WSLOTS, EMBED + SLOT], F32R)
        shared = sb("shared", [P, 2 * SLOT])
        raw_w = shared[:, :].rearrange("p (s n) -> p s n", s=2)
        h1 = shared[:, 0:HID1 // P * TILE].rearrange("p (m n) -> p m n", n=TILE)
        h2 = sb("h2", [P, HID2 // P, TILE])
        prod = sb("prod", [P, 2 * ROUND, TILE])
        half_prod = sb("half_prod", [P, 2, TILE])
        z_sb = sb("z_sb", [P, KTILES, TILE])
        w1_sb = sb("w1_sb", [P, KTILES, HID1])
        w2_sb = sb("w2_sb", [P, HID1 // P, HID2])
        w3_sb = sb("w3_sb", [P, HID2 // P])
        b1_sb = sb("b1_sb", [P, HID1 // P])
        b2_sb = sb("b2_sb", [P, HID2 // P])
        y_sb = sb("y_sb", [1, TILE])
        w_split = nc.dram_tensor("w_split", [P, PAIRS * EMBED], F32)

        main_ps = stack.enter_context(nc.psum_tensor("main_ps", [P, ROUND, TILE], F32))
        z_ps = stack.enter_context(nc.psum_tensor("z_ps", [P, 2, TILE], F32))
        t_ps = stack.enter_context(nc.psum_tensor("t_ps", [P, TILE], F32))
        y_ps = stack.enter_context(nc.psum_tensor("y_ps", [P, TILE], F32))

        const_in = sem("const_in")
        mlp_in = sem("mlp_in")
        ctx_in = sem("ctx_in")
        idx_in = sem("idx_in")
        gathered = [sem(f"gathered{m}") for m in range(DUOS)]
        raw_in = [sem(f"raw_in{s}") for s in range(WSLOTS)]
        stored = [sem(f"stored{s}") for s in range(WSLOTS)]
        w_in = [sem(f"w_in{s}") for s in range(WSLOTS)]
        w_hi = sem("w_hi")
        w_ready = sem("w_ready")
        cleared = sem("cleared")
        transposed = sem("transposed")
        e_hi = sem("e_hi")
        e_kept = sem("e_kept")
        e_lo = sem("e_lo")
        moving = sem("moving")
        mains = sem("mains")
        products = sem("products")
        reduced = sem("reduced")
        z_out = sem("z_out")
        mlp_ps = sem("mlp_ps")
        mlp_act = sem("mlp_act")
        y_out = sem("y_out")
        block = stack.enter_context(nc.Block())

        def duo_done(t, m):
            return DUOS * t + DUOS - m

        def w_columns(c):
            i, q, half = CHUNKS[c]
            g = GROUP_OF[i]
            p = pair_index(i, 2 * q + 1) - 1 - G_FIRST[g]
            return w_sb[:, g % WSLOTS, (p + 1) * EMBED:(p + 3) * EMBED]

        def loop_bank(n):
            return (y_ps, z_ps[:, 1, :])[n % 2]

        def final_bank(n):
            return main_ps[:, n, :] if n < ROUND else (y_ps, t_ps, z_ps[:, 0, :])[n - ROUND]

        def raw_weights(g):
            return raw_w[(LOW, UP)[g % 2], g % WSLOTS // 2, 0:G_PAIRS[g] * EMBED]

        @block.gpsimd
        def _(pool):
            def tile(t, first):
                pool.dma_start(idx[:, :], ids[bass.ds(t, 1)].rearrange("a p n -> (a p) n")).then_inc(idx_in, 16)
                pool.wait_ge(idx_in, 16 * t + 16)
                pool.nop(nofuse=True)
                for m in range(DUOS - 1, -1, -1):
                    if not first:
                        pool.wait_ge(transposed, duo_done(t - 1, m))
                        pool.nop(nofuse=True)
                    for odd in (1, 0):
                        f = 2 * m + odd
                        for s in range(SUBS):
                            pool.indirect_dma_start(
                                out=emb[:, m, s, odd * EMBED:(odd + 1) * EMBED], out_offset=None, in_=tables[f],
                                in_offset=bass.IndirectOffsetOnAxis(ap=idx[:, f * SUBS + s:f * SUBS + s + 1], axis=0),
                            ).then_inc(gathered[m], 16)
                for m in range(DUOS):
                    pool.wait_ge(gathered[m], GATHERS * (t + 1))

            tile(0, True)
            with pool.Fori(1, TILES) as t:
                tile(t, False)

        @block.sync
        def _(sp):
            def load_raw(g):
                if g >= WSLOTS:
                    sp.wait_ge(w_ready, g - WSLOTS + 1)
                src = wsrc[:, G_FIRST[g] * EMBED:(G_FIRST[g] + G_PAIRS[g]) * EMBED]
                sp.dma_start(raw_weights(g), src).then_inc(raw_in[g % WSLOTS], 16)

            def store_split(g):
                sp.wait_ge(w_ready, g + 1)
                cols = slice(G_FIRST[g] * EMBED, (G_FIRST[g] + G_PAIRS[g]) * EMBED)
                sp.dma_start(w_split[:, cols], w_sb[:, g % WSLOTS, EMBED:EMBED + G_PAIRS[g] * EMBED].bitcast(F32))\
                  .then_inc(stored[g % WSLOTS], 16)

            def load_ctx(t, first):
                if not first:
                    sp.wait_ge(reduced, ROUNDS * (t - 1) + HALVES[-1] // ROUND + 1)
                for n in range(2):
                    sp.dma_start(half_prod[0:CTX, n, :], ctx_t[:, bass.ds(t * TILE, TILE)]).then_inc(ctx_in, 16)

            sp.sem_inc(y_out, 16)
            load_raw(0)
            sp.dma_start(const_sb[:, :], const).then_inc(const_in, 16)
            for g in range(1, WSLOTS):
                load_raw(g)
            sp.wait_ge(cleared, 1)
            load_ctx(0, True)
            for g in range(NGROUP):
                store_split(g)
                if g + WSLOTS < NGROUP:
                    load_raw(g + WSLOTS)
                if g == 2:
                    for dst, src in ((w1_sb, w1), (w2_sb, w2)):
                        sp.dma_start(dst[:, :, :], src).then_inc(mlp_in, 16)
                    for dst, src in ((w3_sb, w3), (b1_sb, b1), (b2_sb, b2)):
                        sp.dma_start(dst[:, :], src).then_inc(mlp_in, 16)
            for s in range(WSLOTS):
                sp.wait_ge(stored[s], 16 * (NGROUP // WSLOTS))

            def load_split(t, g):
                prev_t, prev_g = (t, g - WSLOTS) if g >= WSLOTS else (t - 1, g - WSLOTS + NGROUP)
                sp.wait_ge(mains, NCHUNK * prev_t + LAST_OF_STEP[GROUPS[prev_g][-1]] + 1)
                cols = slice(G_FIRST[g] * EMBED, (G_FIRST[g] + G_PAIRS[g]) * EMBED)
                sp.dma_start(w_sb[:, g % WSLOTS, EMBED:EMBED + G_PAIRS[g] * EMBED].bitcast(F32), w_split[:, cols])\
                  .then_inc(w_in[g % WSLOTS], 16)

            def store_y(t):
                sp.wait_ge(mlp_act, MLP_STEPS * (t + 1) + 1)
                sp.dma_start(out[:, bass.ds(t * TILE, TILE)], y_sb[:, :]).then_inc(y_out, 16)

            with sp.Fori(1, TILES) as t:
                for g in range(NGROUP):
                    load_split(t, g)
                    if g == WSLOTS - 2:
                        load_ctx(t, False)
                    if g == WSLOTS + 1:
                        store_y(t - 1)
            store_y(TILES - 1)
            sp.wait_ge(y_out, 16 * (TILES + 1))

        @block.tensor
        def _(pe):
            def transpose_duo(t, m):
                pe.wait_ge(gathered[m], GATHERS * (t + 1))
                for s in range(SUBS):
                    last = nc.tensor.transpose(t_ps[:, s * P:(s + 1) * P], emb[:, m, s, :], ident)
                last.then_inc(transposed, 1)

            def main_products(t, r, first):
                for c in range(ROUND * r, ROUND * r + ROUND):
                    i, q, half = CHUNKS[c]
                    if c == FIRST_OF_STEP[i]:
                        pe.wait_ge(moving, FIELDS * t + FIELDS - i)
                        g = GROUP_OF[i]
                        if i == GROUPS[g][0]:
                            if first:
                                pe.wait_ge(w_ready, g + 1)
                            else:
                                pe.wait_ge(w_in[g % WSLOTS], 16 * ((t - 1) * (NGROUP // WSLOTS) + g // WSLOTS + 1))
                    if c >= ROUND:
                        pe.wait_ge(products, NOPS * t + OPS_THROUGH[c - ROUND])
                    elif not first:
                        pe.wait_ge(products, NOPS * (t - 1) + OPS_THROUGH[c - ROUND + NCHUNK])
                    m, odd = divmod(i, 2)
                    nc.tensor.matmul(main_ps[:, c % ROUND, :], w_columns(c), halves[:, m % MSLOTS, odd, 0, :],
                                     start=True, stop=False)
                    nc.tensor.matmul(main_ps[:, c % ROUND, :], w_columns(c), halves[:, m % MSLOTS, odd, 1, :],
                                     start=False, stop=True).then_inc(mains, 1)

            def reduce_round(t, r):
                kt, s = divmod(r, ROUNDS_KT)
                if s == 0 and not (isinstance(t, int) and KTILES * t + kt < 2):
                    pe.wait_ge(z_out, KTILES * t + kt - 1)
                pe.wait_ge(products, NOPS * t + OPS_THROUGH[ROUND * r + ROUND - 1])
                for g in range(ROUND):
                    c = ROUND * r + g
                    if CHUNKS[c][2]:
                        h = HALVES.index(c)
                        if h < 2:
                            pe.wait_ge(ctx_in, 32 * (t + 1))
                        which, what = half_sel[:, h, :], half_prod[:, h % 2, :]
                    else:
                        which, what = sel[:, 30 - 2 * s:62 - 2 * s], prod[:, c % (2 * ROUND), :]
                    last = nc.tensor.matmul(z_ps[32 * g:32 * g + 32, kt % 2, :], which, what,
                                            start=(s == 0), stop=(s == ROUNDS_KT - 1))
                last.then_inc(reduced, 1)

            def mlp(t, n, bank, in_loop):
                if n == 0:
                    pe.wait_ge(z_out, KTILES * (t + 1))
                layer = 0 if n < HID1 // P else HID1 // P if n < MLP_STEPS - 1 else n
                pe.wait_ge(mlp_act, MLP_STEPS * t + 1 + max(layer, n - 1 if in_loop else 0))
                if n < HID1 // P:
                    w, x, m = w1_sb, z_sb, n
                elif n < MLP_STEPS - 1:
                    w, x, m = w2_sb, h1, n - HID1 // P
                else:
                    for k in range(HID2 // P):
                        last = nc.tensor.matmul(bank[0:1, :], w3_sb[:, k:k + 1], h2[:, k, :],
                                                start=(k == 0), stop=(k == HID2 // P - 1))
                    last.then_inc(mlp_ps, 1)
                    return
                for k in range(KTILES):
                    last = nc.tensor.matmul(bank[:, :], w[:, k, m * P:(m + 1) * P], x[:, k, :],
                                            start=(k == 0), stop=(k == KTILES - 1))
                last.then_inc(mlp_ps, 1)

            def tile(t, first=False, last=False):
                for kind, n in order_events(first, last):
                    if kind == "duo":
                        at, m = (t, n) if n >= 0 else (t + 1, n + DUOS)
                        if not (first and n == DUOS - 1):
                            pe.wait_ge(e_lo, duo_done(at, m) - 1)
                        transpose_duo(at, m)
                    elif kind == "round":
                        main_products(t, n, first)
                    elif kind == "reduce":
                        reduce_round(t, n) if n >= 0 else reduce_round(t - 1, ROUNDS - 1)
                    elif kind == "mlp":
                        mlp(t - 1, n, loop_bank(n), True)

            pe.wait_ge(const_in, 16)
            pe.wait_ge(cleared, 2)
            tile(0, first=True)
            pe.wait_ge(mlp_in, 5 * 16)
            with pe.Fori(1, TILES - 1) as t:
                tile(t)
            tile(TILES - 1, last=True)
            reduce_round(TILES - 1, ROUNDS - 1)
            for n in range(MLP_STEPS):
                mlp(TILES - 1, n, final_bank(n), False)

        @block.vector
        def _(dve):
            nc.vector.memset(half_prod[LOW, :, :], 0.0).then_inc(cleared, 1)
            nc.vector.memset(w_sb[:, :, 0:EMBED].bitcast(F32), 0.0).then_inc(cleared, 1)

            def low_weights(g):
                dve.wait_ge(w_hi, g + 1)
                slot = w_sb[:, g % WSLOTS, EMBED:EMBED + G_PAIRS[g] * EMBED]
                high, low = (LOW, UP) if g % 2 == 0 else (UP, LOW)
                nc.vector.tensor_tensor(slot[low, :], raw_weights(g), slot[high, :].bitcast(F32), ALU.subtract)\
                  .then_inc(w_ready, 1)

            def low_duo(t, m):
                dve.wait_ge(e_hi, duo_done(t, m))
                dve.wait_ge(e_kept, duo_done(t, m))
                nc.vector.tensor_tensor(halves[:, m % MSLOTS, 0, 1, :], t_ps[:, :],
                                        halves[:, m % MSLOTS, 0, 0, :].bitcast(F32), ALU.subtract).then_inc(e_lo, 1)

            def multiply(t, r, first):
                for c, k in OPS:
                    if c // ROUND != r:
                        continue
                    i, q, half = CHUNKS[c]
                    dve.wait_ge(mains, NCHUNK * t + c + k)
                    if half:
                        before = HALVES.index(c) - 2
                        if before >= 0:
                            dve.wait_ge(reduced, ROUNDS * t + HALVES[before] // ROUND + 1)
                        elif not first:
                            dve.wait_ge(reduced, ROUNDS * (t - 1) + HALVES[before] // ROUND + 1)
                        nc.vector.tensor_tensor(half_prod[UP, HALVES.index(c) % 2, :], main_ps[UP, c % ROUND, :],
                                                e_t[UP, q, :], ALU.mult).then_inc(products, 1)
                        continue
                    if r >= 2 or not first:
                        dve.wait_ge(reduced, ROUNDS * t + r - 1)
                    a, s = c % ROUND, c % (2 * ROUND)
                    nc.vector.tensor_tensor(prod[:, s:s + k, :], main_ps[:, a:a + k, :], e_t[:, q:q + k, :],
                                            ALU.mult).then_inc(products, 1)

            def tile(t, first=False, last=False):
                for kind, n in order_events(first, last):
                    if kind == "wlow":
                        low_weights(n)
                    elif kind == "split":
                        low_duo(*((t, n) if n >= 0 else (t + 1, n + DUOS)))
                    elif kind == "round":
                        multiply(t, n, first)

            tile(0, first=True)
            with dve.Fori(1, TILES - 1) as t:
                tile(t)
            tile(TILES - 1, last=True)

        @block.scalar
        def _(act):
            def copy(dst, src):
                return nc.scalar.activation(dst, src, ACT.Copy)

            def high_weights(g):
                act.wait_ge(raw_in[g % WSLOTS], 16 * (g // WSLOTS + 1))
                if g >= WSLOTS:
                    act.wait_ge(mains, LAST_OF_STEP[GROUPS[g - WSLOTS][-1]] + 1)
                    act.wait_ge(stored[g % WSLOTS], 16 * (g // WSLOTS))
                copy(w_sb[(LOW, UP)[g % 2], g % WSLOTS, EMBED:EMBED + G_PAIRS[g] * EMBED], raw_weights(g)).then_inc(w_hi, 1)

            def high_duo(t, m, first):
                act.wait_ge(transposed, duo_done(t, m))
                if m + MSLOTS < DUOS:
                    act.wait_ge(mains, NCHUNK * t + LAST_OF_STEP[2 * (m + MSLOTS)] + 1)
                elif not first:
                    act.wait_ge(mains, NCHUNK * (t - 1) + LAST_OF_STEP[2 * (m + MSLOTS - DUOS)] + 1)
                copy(halves[:, m % MSLOTS, 0, 0, :], t_ps[:, :]).then_inc(e_hi, 1)
                if not first:
                    last = max(c for c, ch in enumerate(CHUNKS) if ch[1] == m)
                    act.wait_ge(products, NOPS * (t - 1) + OPS_THROUGH[last])
                copy(e_t[:, m, :], t_ps[:, :]).then_inc(e_kept, 1)

            def spread_duo(t, m):
                act.wait_ge(e_lo, duo_done(t, m))
                even, odd = halves[:, m % MSLOTS, 0], halves[:, m % MSLOTS, 1]
                for rows in (LOW, UP):
                    last = copy(odd[rows], even[UP].bitcast(F32))
                last.then_inc(moving, 1)
                act.wait_ge(moving, FIELDS * t + FIELDS - 1 - 2 * m)
                copy(even[UP], even[LOW].bitcast(F32)).then_inc(moving, 1)

            def z_tile(t, kt):
                act.wait_ge(reduced, ROUNDS * t + ROUNDS_KT * (kt + 1))
                if kt == 0 and not (isinstance(t, int) and t == 0):
                    act.wait_ge(mlp_ps, MLP_STEPS * (t - 1) + HID1 // P)
                copy(z_sb[:, kt, :], z_ps[:, kt % 2, :]).then_inc(z_out, 1)

            def mlp(t, n, bank):
                act.wait_ge(mlp_ps, MLP_STEPS * t + n + 1)
                if n < HID1 // P:
                    ins = nc.scalar.activation(h1[:, n, :], bank[:, :], ACT.Relu, bias=b1_sb[:, n:n + 1])
                elif n < MLP_STEPS - 1:
                    m = n - HID1 // P
                    ins = nc.scalar.activation(h2[:, m, :], bank[:, :], ACT.Relu, bias=b2_sb[:, m:m + 1])
                else:
                    act.wait_ge(y_out, 16 * (t + 1))
                    ins = copy(y_sb[:, :], bank[0:1, :])
                ins.then_inc(mlp_act, 1)

            def tile(t, first=False, last=False):
                for kind, n in order_events(first, last):
                    if kind == "whigh":
                        high_weights(n)
                    elif kind == "duo" and n >= 0:
                        high_duo(t, n, first)
                    elif kind == "duo":
                        high_duo(t + 1, n + DUOS, False)
                    elif kind == "split":
                        spread_duo(*((t, n) if n >= 0 else (t + 1, n + DUOS)))
                    elif kind == "zout":
                        z_tile(t, n) if n >= 0 else z_tile(t - 1, KTILES - 1)
                    elif kind == "mlp":
                        mlp(t - 1, n, loop_bank(n))

            act.sem_inc(mlp_act, 1)
            tile(0, first=True)
            act.wait_ge(mlp_in, 5 * 16)
            with act.Fori(1, TILES - 1) as t:
                tile(t)
            tile(TILES - 1, last=True)
            z_tile(TILES - 1, KTILES - 1)
            for n in range(MLP_STEPS):
                mlp(TILES - 1, n, final_bank(n))


def kernel(**inputs):
    import numpy as np
    import concourse.bacc as bacc
    from concourse.bass_utils import run_bass_kernel_spmd

    nc = bacc.Bacc("TRN2", target_bir_lowering=False, num_devices=1)

    const = np.zeros((P, P + 62 + 32 * CTX), np.float32)
    const[:, :P] = np.eye(P, dtype=np.float32)
    const[:EMBED, P + 30] = 1
    const[EMBED:, P + 31] = 1
    for h, c in enumerate(HALVES):
        s = c // ROUND % ROUNDS_KT
        const[h, P + 62 + 32 * h + 2 * s] = 1
        const[EMBED:, P + 62 + 32 * h + 2 * s + 1] = 1

    a = {k: np.asarray(v) for k, v in inputs.items()}
    arrays = {
        "const": const,
        "ids": a["ids"].reshape(TILES, SUBS, P, FIELDS).transpose(0, 2, 3, 1).reshape(TILES, P, FIELDS * SUBS),
        "w": a["L0_rec_w"].transpose(1, 0, 2).reshape(EMBED, PAIRS * EMBED),
        "w1": a["W_top1"][w1_rows()].reshape(KTILES, P, HID1).transpose(1, 0, 2),
        "w2": a["W_top2"].reshape(HID1 // P, P, HID2).transpose(1, 0, 2),
        "w3": a["W_top3"].reshape(HID2 // P, P).T,
        "b1": a["b_top1"].reshape(HID1 // P, P).T,
        "b2": a["b_top2"].reshape(HID2 // P, P).T,
        "ctx": a["dense_ctx"].T,
    }
    for f in range(FIELDS):
        arrays[f"tbl_{f}"] = a[f"tbl_{f}"]
    arrays = {f"in_{k}": np.ascontiguousarray(v) for k, v in arrays.items()}
    ap = {k: nc.dram_tensor(k, v.shape, mybir.dt.from_np(v.dtype), kind="ExternalInput").ap()
          for k, v in arrays.items()}
    out = nc.dram_tensor("out_y", (1, BATCH), mybir.dt.float32, kind="ExternalOutput").ap()
    dlrm_tower(nc, ap["in_const"], ap["in_ids"], ap["in_w"], ap["in_w1"], ap["in_w2"], ap["in_w3"], ap["in_b1"],
               ap["in_b2"], ap["in_ctx"], [ap[f"in_tbl_{f}"] for f in range(FIELDS)], out)
    r = run_bass_kernel_spmd(nc, [arrays], core_ids=[0])
    return r.results[0]["out_y"].reshape(BATCH, 1)
```

```python
from contextlib import ExitStack

import concourse.bass as bass
from concourse import mybir

BATCH, FIELDS, EMBED, CTX = 2048, 32, 64, 16
HID1, HID2 = 512, 256
P = 128
TILE = 512
TILES = BATCH // TILE
SUBS = TILE // P
DUOS = FIELDS // 2
PAIRS = FIELDS * (FIELDS - 1) // 2


def pair_index(i, j):
    return i * (FIELDS - 1) - i * (i - 1) // 2 + j - i - 1


def order_chunks():
    chunks, ops = [], []
    todo = []
    for i in range(FIELDS - 2, -1, -1):
        if i < FIELDS - 2:
            todo.append([i, (i + 1) // 2 + (i % 2 == 0), DUOS - 1, i % 4 == 0])
    while todo:
        step = todo[0]
        if len(todo) == 2 and todo[1][2] > step[2]:
            step = todo[1]
        i, low, top, twin = step
        c = len(chunks)
        if twin and (c % 4 == 3 or top < low):
            chunks.append((i, i // 2, True))
            ops.append((c, 1))
            step[3] = False
        elif top == low or c % 4 == 3:
            chunks.append((i, top, False))
            ops.append((c, 1))
            step[2] -= 1
        else:
            chunks += [(i, top - 1, False), (i, top, False)]
            ops.append((c, 2))
            step[2] -= 2
        if step[2] < low and not step[3]:
            todo.remove(step)
    return chunks, ops


CHUNKS, OPS = order_chunks()
NCHUNK = len(CHUNKS)
ROUND = 4
ROUNDS = NCHUNK // ROUND
ROUNDS_KT = P // (2 * ROUND)
KTILES = -(-ROUNDS // ROUNDS_KT)
CTX_COL = 2 * (ROUNDS % ROUNDS_KT)
assert ROUND * (2 * ROUNDS_KT - CTX_COL) == CTX
USED_BY = {i: [c for c, (s, _, twin) in enumerate(CHUNKS) if s == i or (twin and s + 2 == i)] for i in range(FIELDS - 1)}
LAST_OF_STEP = {i: max(USED_BY[i]) for i in range(FIELDS - 1)}
FIRST_OF_STEP = {i: min(USED_BY[i]) for i in range(FIELDS - 1)}
LAST_OF_DUO = [max(LAST_OF_STEP[i] for i in (2 * m, 2 * m + 1) if i < FIELDS - 1) for m in range(DUOS)]
TWIN_OF_DUO = [CHUNKS.index((m // 2 * 4, m // 2 * 2, True)) for m in range(DUOS)]
LAST_OF_Q = [max(c for c, ch in enumerate(CHUNKS) if ch[1] == q) for q in range(DUOS)]
OPS_THROUGH = {}
for _n, (_c, _k) in enumerate(OPS):
    for _d in range(_k):
        OPS_THROUGH[_c + _d] = _n + 1
NOPS = len(OPS)


SLOT_PAIRS = 31


def order_groups():
    groups, cur = [], []
    for i in range(FIELDS - 2, -1, -1):
        if cur and sum(FIELDS - 1 - k for k in cur) + FIELDS - 1 - i > SLOT_PAIRS:
            groups.append(cur)
            cur = []
        cur.append(i)
    return groups + [cur]


GROUPS = order_groups()
NGROUP = len(GROUPS)
GROUP_OF = {i: g for g, steps in enumerate(GROUPS) for i in steps}
G_FIRST = [pair_index(steps[-1], steps[-1] + 1) for steps in GROUPS]
LAST_OF_GROUP = [max(LAST_OF_STEP[i] for i in steps) for steps in GROUPS]
FIRST_OF_GROUP = [min(FIRST_OF_STEP[i] for i in steps) for steps in GROUPS]
G_PAIRS = [sum(FIELDS - 1 - i for i in steps) for steps in GROUPS]
WSLOTS = 4
STAGES = 3
HALF_PAIRS = (SLOT_PAIRS + 1) // 2
SPLIT_AHEAD = 8
DUO_AHEAD = {True: 3, False: 5}
assert NGROUP % WSLOTS == 0
MSLOTS = 4
TSLOTS = 3
MLP_LOAD_GROUP = 8
MLP_STEPS = HID1 // P + HID2 // P + 1
GATHERS = 16 * 2 * SUBS


def z_row(c, upper):
    r, g = divmod(c, ROUND)
    kt, s = divmod(r, ROUNDS_KT)
    return kt * P + 32 * g + 2 * s + upper


def w1_rows():
    rows = [0] * (KTILES * P)
    for c, (i, q, twin) in enumerate(CHUNKS):
        rows[z_row(c, 0)] = pair_index(i + 2, i + 3) if twin else pair_index(i, 2 * q)
        rows[z_row(c, 1)] = pair_index(i, 2 * q + 1)
    n = CTX // ROUND
    for f in range(CTX):
        rows[(KTILES - 1) * P + 32 * (f // n) + CTX_COL + f % n] = PAIRS + f
    return rows


FIRST_OF_DUO = {m: FIRST_OF_STEP[min(2 * m + 1, FIELDS - 2)] for m in range(DUOS)}
AHEAD = 3


def order_events(first, last):
    ev, duos, weights, blocks = [], [], [], []
    if first:
        ev += [(kind, g) for g in range(STAGES) for kind in ("whigh", "wlow")]
        for n in range(AHEAD):
            ev += [("duo", DUOS - 1 - n), ("split", DUOS - 1 - n)]
    else:
        blocks = [("mlp", n) for n in range(MLP_STEPS)]
    for m in range(DUOS - 1 - AHEAD, -1, -1):
        free = LAST_OF_DUO[m + MSLOTS] // ROUND if m + MSLOTS < DUOS else -1
        soon = FIRST_OF_DUO[m] // ROUND - DUO_AHEAD[first]
        duos.append((max(free, soon), m))
    if not last:
        for m in range(DUOS - 1, DUOS - 1 - AHEAD, -1):
            free = max(LAST_OF_Q[m], TWIN_OF_DUO[m % (2 * TSLOTS)] if m >= DUOS - 2 * TSLOTS else 0)
            duos.append((free // ROUND, m - DUOS))
    if first:
        for g in range(STAGES, NGROUP):
            past = g - STAGES - 1 - WSLOTS
            free = LAST_OF_GROUP[past] // ROUND if past >= 0 else -1
            weights.append((max(free, FIRST_OF_GROUP[g] // ROUND - SPLIT_AHEAD), g))
    split, low, busy = [], [], -2
    for r in range(-1, ROUNDS):
        if r >= 0:
            ev.append(("round", r))
            if r or not first:
                ev.append(("reduce", r - 1))
            if r % ROUNDS_KT == 0 and (r or not first):
                ev.append(("zout", r // ROUNDS_KT - 1))
            ev += split + low
            split, low = [], []
            if blocks:
                ev.append(blocks.pop(0))
        if duos and duos[0][0] <= r and r - busy >= (2 if duos[0][1] < 0 else 1) and not (first and split):
            busy = r
            m = duos.pop(0)[1]
            ev.append(("duo", m))
            split = [("split", m)]
        if weights and weights[0][0] <= r:
            g = weights.pop(0)[1]
            ev.append(("whigh", g))
            low = [("wlow", g)]
    return ev + split + low + [("duo", m) if k == 0 else ("split", m) for _, m in duos for k in (0, 1)]


def dlrm_tower(nc, const, ids, wsrc, w1, w2, w3, b1, b2, ctx_t, tables, out):
    F32, F32R, I32 = mybir.dt.float32, mybir.dt.float32r, mybir.dt.int32
    ALU, ACT = mybir.AluOpType, mybir.ActivationFunctionType
    SLOT, HALF = SLOT_PAIRS * EMBED, HALF_PAIRS * EMBED
    LOW, UP = slice(0, EMBED), slice(EMBED, P)

    with ExitStack() as stack:
        def sb(name, shape, dt=F32):
            return stack.enter_context(nc.sbuf_tensor(name, shape, dt))

        def sem(name):
            return stack.enter_context(nc.semaphore(name))

        const_sb = sb("const_sb", [P, const.shape[1]])
        ident = const_sb[:, 0:P]
        sel = const_sb[:, P:P + 62]
        ctx_sel = const_sb[0:CTX, P + 62:].rearrange("p (g n) -> p g n", n=32)
        idx = sb("idx", [P, FIELDS * SUBS], I32)
        emb = sb("emb", [P, DUOS, SUBS, P])
        e_t = sb("e_t", [P, DUOS, TILE])
        halves = sb("halves", [P, MSLOTS, 2, 2, TILE], F32R)
        e_twin = sb("e_twin", [P, TSLOTS, TILE])
        w_sb = sb("w_sb", [P, WSLOTS, EMBED + SLOT], F32R)
        shared = sb("shared", [P, STAGES * HALF])
        raw_w = shared[:, :].rearrange("p (s n) -> p s n", s=STAGES)
        high_w = sb("high_w", [P, STAGES, HALF], F32R)
        h1 = shared[:, 0:HID1 // P * TILE].rearrange("p (m n) -> p m n", n=TILE)
        h2 = sb("h2", [P, HID2 // P, TILE])
        prod = sb("prod", [P, 2 * ROUND, TILE])
        ctx_sb = sb("ctx_sb", [CTX, TILE])
        z_sb = sb("z_sb", [P, KTILES, TILE])
        w1_sb = sb("w1_sb", [P, KTILES, HID1])
        w2_sb = sb("w2_sb", [P, HID1 // P, HID2])
        w3_sb = sb("w3_sb", [P, HID2 // P])
        b1_sb = sb("b1_sb", [P, HID1 // P])
        b2_sb = sb("b2_sb", [P, HID2 // P])
        y_sb = sb("y_sb", [1, TILE])
        w_split = nc.dram_tensor("w_split", [P, PAIRS * EMBED], F32)

        main_ps = stack.enter_context(nc.psum_tensor("main_ps", [P, ROUND, TILE], F32))
        z_ps = stack.enter_context(nc.psum_tensor("z_ps", [P, 2, TILE], F32))
        t_ps = stack.enter_context(nc.psum_tensor("t_ps", [P, TILE], F32))
        y_ps = stack.enter_context(nc.psum_tensor("y_ps", [P, TILE], F32))

        const_in = sem("const_in")
        mlp_in = sem("mlp_in")
        ctx_in = sem("ctx_in")
        idx_in = sem("idx_in")
        gathered = [sem(f"gathered{m}") for m in range(DUOS)]
        raw_in = [sem(f"raw_in{s}") for s in range(STAGES)]
        stored = [sem(f"stored{s}") for s in range(STAGES)]
        w_in = [sem(f"w_in{s}") for s in range(WSLOTS)]
        cleared = sem("cleared")
        w_hi = sem("w_hi")
        w_lo = sem("w_lo")
        transposed = sem("transposed")
        e_hi = sem("e_hi")
        e_kept = sem("e_kept")
        e_lo = sem("e_lo")
        moving = sem("moving")
        mains = sem("mains")
        products = sem("products")
        reduced = sem("reduced")
        z_out = sem("z_out")
        mlp_ps = sem("mlp_ps")
        mlp_act = sem("mlp_act")
        y_out = sem("y_out")
        block = stack.enter_context(nc.Block())

        def duo_done(t, m):
            return DUOS * t + DUOS - m

        def w_columns(i, j, n, before=0):
            g = GROUP_OF[i]
            p = pair_index(i, j) - G_FIRST[g] - before
            return w_sb[:, g % WSLOTS, (p + 1) * EMBED:(p + 1 + n) * EMBED]

        def loop_bank(n):
            return (y_ps, z_ps[:, 1, :])[n % 2]

        def final_bank(n):
            return main_ps[:, n, :] if n < ROUND else (y_ps, t_ps, z_ps[:, 0, :])[n - ROUND]

        def group_halves(g):
            n = (G_PAIRS[g] + 1) // 2
            return n, ((LOW, G_FIRST[g], 0), (UP, G_FIRST[g] + G_PAIRS[g] - n, 2 * n - G_PAIRS[g]))

        @block.gpsimd
        def _(pool):
            def tile(t, first):
                pool.dma_start(idx[:, :], ids[bass.ds(t, 1)].rearrange("a p n -> (a p) n")).then_inc(idx_in, 16)
                pool.wait_ge(idx_in, 16 * t + 16)
                pool.nop(nofuse=True)
                for m in range(DUOS - 1, -1, -1):
                    if not first:
                        pool.wait_ge(transposed, duo_done(t - 1, m))
                        pool.nop(nofuse=True)
                    for odd in (1, 0):
                        f = 2 * m + odd
                        for s in range(SUBS):
                            pool.indirect_dma_start(
                                out=emb[:, m, s, odd * EMBED:(odd + 1) * EMBED], out_offset=None, in_=tables[f],
                                in_offset=bass.IndirectOffsetOnAxis(ap=idx[:, f * SUBS + s:f * SUBS + s + 1], axis=0),
                            ).then_inc(gathered[m], 16)
                for m in range(DUOS):
                    pool.wait_ge(gathered[m], GATHERS * (t + 1))

            tile(0, True)
            with pool.Fori(1, TILES) as t:
                tile(t, False)

        @block.sync
        def _(sp):
            def load_raw(g):
                if g >= STAGES:
                    sp.wait_ge(stored[g % STAGES], 4 * 16 * (g // STAGES))
                n, parts = group_halves(g)
                for rows, first, _ in parts:
                    sp.dma_start(raw_w[rows, g % STAGES, 0:n * EMBED], wsrc[:, first * EMBED:(first + n) * EMBED])\
                      .then_inc(raw_in[g % STAGES], 16)

            def store_split(g):
                n, parts = group_halves(g)
                for made, dst_rows, src in ((w_hi, LOW, high_w), (w_lo, UP, raw_w)):
                    sp.wait_ge(made, g + 1)
                    for rows, first, skip in parts:
                        src_part = src[rows, g % STAGES, skip * EMBED:n * EMBED]
                        sp.dma_start(w_split[dst_rows, (first + skip) * EMBED:(first + n) * EMBED],
                                     src_part.bitcast(F32) if made is w_hi else src_part)\
                          .then_inc(stored[g % STAGES], 16)

            def load_ctx(t, first):
                if not first:
                    sp.wait_ge(reduced, ROUNDS * t)
                sp.dma_start(ctx_sb[:, :], ctx_t[:, bass.ds(t * TILE, TILE)]).then_inc(ctx_in, 16)

            sp.sem_inc(y_out, 16)
            load_raw(0)
            sp.dma_start(const_sb[:, :], const).then_inc(const_in, 16)
            for g in range(1, STAGES):
                load_raw(g)
            load_ctx(0, True)

            def load_split(t, g, first=False):
                if g >= WSLOTS or not first:
                    prev_t, prev_g = (t, g - WSLOTS) if g >= WSLOTS else (t - 1, g - WSLOTS + NGROUP)
                    sp.wait_ge(mains, NCHUNK * prev_t + LAST_OF_GROUP[prev_g] + 1)
                cols = slice(G_FIRST[g] * EMBED, (G_FIRST[g] + G_PAIRS[g]) * EMBED)
                sp.dma_start(w_sb[:, g % WSLOTS, EMBED:EMBED + G_PAIRS[g] * EMBED].bitcast(F32), w_split[:, cols])\
                  .then_inc(w_in[g % WSLOTS], 16)

            for g in range(NGROUP):
                store_split(g)
                if g + STAGES < NGROUP:
                    load_raw(g + STAGES)
                sp.wait_ge(stored[g % STAGES], 4 * 16 * (g // STAGES + 1))
                load_split(0, g, first=True)
                if g == MLP_LOAD_GROUP:
                    for dst, src in ((w1_sb, w1), (w2_sb, w2)):
                        sp.dma_start(dst[:, :, :], src).then_inc(mlp_in, 16)
                    for dst, src in ((w3_sb, w3), (b1_sb, b1), (b2_sb, b2)):
                        sp.dma_start(dst[:, :], src).then_inc(mlp_in, 16)

            def store_y(t):
                sp.wait_ge(mlp_act, MLP_STEPS * (t + 1) + 1)
                sp.dma_start(out[:, bass.ds(t * TILE, TILE)], y_sb[:, :]).then_inc(y_out, 16)

            with sp.Fori(1, TILES) as t:
                for g in range(NGROUP):
                    load_split(t, g)
                    if g == WSLOTS - 2:
                        load_ctx(t, False)
                    if g == WSLOTS + 1:
                        store_y(t - 1)
            store_y(TILES - 1)
            sp.wait_ge(y_out, 16 * (TILES + 1))

        @block.tensor
        def _(pe):
            def transpose_duo(t, m):
                pe.wait_ge(gathered[m], GATHERS * (t + 1))
                for s in range(SUBS):
                    last = nc.tensor.transpose(t_ps[:, s * P:(s + 1) * P], emb[:, m, s, :], ident)
                last.then_inc(transposed, 1)

            def main_products(t, r, first):
                for c in range(ROUND * r, ROUND * r + ROUND):
                    i, q, twin = CHUNKS[c]
                    if c == FIRST_OF_STEP[i]:
                        pe.wait_ge(moving, FIELDS * t + FIELDS - i)
                    for g in range(NGROUP):
                        if c == FIRST_OF_GROUP[g]:
                            pe.wait_ge(w_in[g % WSLOTS], 16 * (t * (NGROUP // WSLOTS) + g // WSLOTS + 1))
                    if c >= ROUND:
                        pe.wait_ge(products, NOPS * t + OPS_THROUGH[c - ROUND])
                    elif not first:
                        pe.wait_ge(products, NOPS * (t - 1) + OPS_THROUGH[c - ROUND + NCHUNK])
                    m, odd = divmod(i, 2)
                    bank = main_ps[:, c % ROUND, :]
                    w = w_columns(i, 2 * q + 1, 2, before=1) if twin else w_columns(i, 2 * q, 2)
                    for part in range(2):
                        ins = nc.tensor.matmul(bank, w, halves[:, m % MSLOTS, odd, part, :],
                                               start=(part == 0), stop=(part == 1))
                    if twin:
                        for part in range(2):
                            ins = nc.tensor.matmul(bank[LOW, :], w_columns(i + 2, i + 3, 1),
                                                   halves[:, (m + 1) % MSLOTS, 0, part, :],
                                                   start=(part == 0), stop=(part == 1))
                    ins.then_inc(mains, 1)

            def reduce_round(t, r):
                kt, s = divmod(r, ROUNDS_KT)
                if s == 0 and not (isinstance(t, int) and KTILES * t + kt < 2):
                    pe.wait_ge(z_out, KTILES * t + kt - 1)
                pe.wait_ge(products, NOPS * t + OPS_THROUGH[ROUND * r + ROUND - 1])
                if r == ROUNDS - 1:
                    pe.wait_ge(ctx_in, 16 * (t + 1))
                bank = z_ps[:, kt % 2, :]
                for g in range(ROUND):
                    last = nc.tensor.matmul(bank[32 * g:32 * g + 32, :], sel[:, 30 - 2 * s:62 - 2 * s],
                                            prod[:, (ROUND * r + g) % (2 * ROUND), :],
                                            start=(s == 0), stop=(s == ROUNDS_KT - 1))
                if r == ROUNDS - 1:
                    for g in range(ROUND):
                        last = nc.tensor.matmul(bank[32 * g:32 * g + 32, :], ctx_sel[:, g, :], ctx_sb[:, :],
                                                start=False, stop=True)
                last.then_inc(reduced, 1)

            def mlp(t, n, bank, in_loop):
                done = MLP_STEPS * t + 1
                if n < HID1 // P:
                    w, x, m = w1_sb, z_sb, n
                elif n < MLP_STEPS - 1:
                    w, x, m = w2_sb, h1, n - HID1 // P
                else:
                    w, x, m = w3_sb, h2, 0
                if in_loop:
                    pe.wait_ge(mlp_act, done + max(0, n - 1))
                depth = HID2 // P if x is h2 else KTILES
                for k in range(depth):
                    if n == 0 and k in (0, KTILES - 1):
                        pe.wait_ge(z_out, KTILES * (t + 1) - (k == 0))
                    if n == HID1 // P:
                        pe.wait_ge(mlp_act, done + k + 1)
                    if x is h2:
                        pe.wait_ge(mlp_act, done + HID1 // P + k + 1)
                        lhs, dst = w3_sb[:, k:k + 1], bank[0:1, :]
                    else:
                        lhs, dst = w[:, k, m * P:(m + 1) * P], bank[:, :]
                    last = nc.tensor.matmul(dst, lhs, x[:, k, :], start=(k == 0), stop=(k == depth - 1))
                last.then_inc(mlp_ps, 1)

            def tile(t, first=False, last=False):
                for kind, n in order_events(first, last):
                    if kind == "duo":
                        at, m = (t, n) if n >= 0 else (t + 1, n + DUOS)
                        if not (first and n == DUOS - 1):
                            pe.wait_ge(e_lo, duo_done(at, m) - 1)
                        transpose_duo(at, m)
                    elif kind == "round":
                        main_products(t, n, first)
                    elif kind == "reduce":
                        reduce_round(t, n) if n >= 0 else reduce_round(t - 1, ROUNDS - 1)
                    elif kind == "mlp":
                        mlp(t - 1, n, loop_bank(n), True)

            pe.wait_ge(const_in, 16)
            pe.wait_ge(cleared, 1)
            tile(0, first=True)
            pe.wait_ge(mlp_in, 5 * 16)
            with pe.Fori(1, TILES - 1) as t:
                tile(t)
            tile(TILES - 1, last=True)
            reduce_round(TILES - 1, ROUNDS - 1)
            for n in range(MLP_STEPS):
                mlp(TILES - 1, n, final_bank(n), False)

        @block.vector
        def _(dve):
            nc.vector.memset(w_sb[:, :, 0:EMBED].bitcast(F32), 0.0).then_inc(cleared, 1)

            def low_weights(g):
                dve.wait_ge(w_hi, g + 1)
                raw = raw_w[:, g % STAGES, 0:group_halves(g)[0] * EMBED]
                high = high_w[:, g % STAGES, 0:group_halves(g)[0] * EMBED]
                nc.vector.tensor_tensor(raw, raw, high.bitcast(F32), ALU.subtract).then_inc(w_lo, 1)

            def low_duo(t, m):
                dve.wait_ge(e_hi, duo_done(t, m))
                dve.wait_ge(e_kept, duo_done(t, m))
                nc.vector.tensor_tensor(halves[:, m % MSLOTS, 0, 1, :], t_ps[:, :],
                                        halves[:, m % MSLOTS, 0, 0, :].bitcast(F32), ALU.subtract).then_inc(e_lo, 1)

            def multiply(t, r, first):
                for c, k in OPS:
                    if c // ROUND != r:
                        continue
                    i, q, twin = CHUNKS[c]
                    dve.wait_ge(mains, NCHUNK * t + c + k)
                    if r >= 2 or not first:
                        dve.wait_ge(reduced, ROUNDS * t + r - 1)
                    a, s = c % ROUND, c % (2 * ROUND)
                    e_j = e_twin[:, q // 2 % TSLOTS:q // 2 % TSLOTS + 1, :] if twin else e_t[:, q:q + k, :]
                    nc.vector.tensor_tensor(prod[:, s:s + k, :], main_ps[:, a:a + k, :], e_j, ALU.mult)\
                      .then_inc(products, 1)

            def tile(t, first=False, last=False):
                for kind, n in order_events(first, last):
                    if kind == "wlow":
                        low_weights(n)
                    elif kind == "split":
                        low_duo(*((t, n) if n >= 0 else (t + 1, n + DUOS)))
                    elif kind == "round":
                        multiply(t, n, first)

            tile(0, first=True)
            with dve.Fori(1, TILES - 1) as t:
                tile(t)
            tile(TILES - 1, last=True)

        @block.scalar
        def _(act):
            def copy(dst, src):
                return nc.scalar.activation(dst, src, ACT.Copy)

            def high_weights(g):
                act.wait_ge(raw_in[g % STAGES], 2 * 16 * (g // STAGES + 1))
                n = group_halves(g)[0] * EMBED
                copy(high_w[:, g % STAGES, 0:n], raw_w[:, g % STAGES, 0:n]).then_inc(w_hi, 1)

            def high_duo(t, m, first):
                act.wait_ge(transposed, duo_done(t, m))
                if m + MSLOTS < DUOS:
                    act.wait_ge(mains, NCHUNK * t + LAST_OF_DUO[m + MSLOTS] + 1)
                elif not first:
                    act.wait_ge(mains, NCHUNK * (t - 1) + LAST_OF_DUO[m + MSLOTS - DUOS] + 1)
                copy(halves[:, m % MSLOTS, 0, 0, :], t_ps[:, :]).then_inc(e_hi, 1)
                if not first:
                    act.wait_ge(products, NOPS * (t - 1) + OPS_THROUGH[LAST_OF_Q[m]])
                copy(e_t[:, m, :], t_ps[:, :])
                if m + 2 * TSLOTS < DUOS:
                    act.wait_ge(products, NOPS * t + OPS_THROUGH[TWIN_OF_DUO[m + 2 * TSLOTS]])
                elif not first:
                    act.wait_ge(products, NOPS * (t - 1) + OPS_THROUGH[TWIN_OF_DUO[m % (2 * TSLOTS)]])
                copy(e_twin[(UP, LOW)[m % 2], m // 2 % TSLOTS, :], t_ps[UP, :]).then_inc(e_kept, 1)

            def spread_duo(t, m):
                act.wait_ge(e_lo, duo_done(t, m))
                even, odd = halves[:, m % MSLOTS, 0], halves[:, m % MSLOTS, 1]
                for rows in (LOW, UP):
                    last = copy(odd[rows], even[UP].bitcast(F32))
                last.then_inc(moving, 1)
                act.wait_ge(moving, FIELDS * t + FIELDS - 1 - 2 * m)
                copy(even[UP], even[LOW].bitcast(F32)).then_inc(moving, 1)

            def z_tile(t, kt):
                act.wait_ge(reduced, ROUNDS * t + min(ROUNDS_KT * (kt + 1), ROUNDS))
                if kt == 0 and not (isinstance(t, int) and t == 0):
                    act.wait_ge(mlp_ps, MLP_STEPS * (t - 1) + HID1 // P)
                copy(z_sb[:, kt, :], z_ps[:, kt % 2, :]).then_inc(z_out, 1)

            def mlp(t, n, bank):
                act.wait_ge(mlp_ps, MLP_STEPS * t + n + 1)
                if n < HID1 // P:
                    ins = nc.scalar.activation(h1[:, n, :], bank[:, :], ACT.Relu, bias=b1_sb[:, n:n + 1])
                elif n < MLP_STEPS - 1:
                    m = n - HID1 // P
                    ins = nc.scalar.activation(h2[:, m, :], bank[:, :], ACT.Relu, bias=b2_sb[:, m:m + 1])
                else:
                    act.wait_ge(y_out, 16 * (t + 1))
                    ins = copy(y_sb[:, :], bank[0:1, :])
                ins.then_inc(mlp_act, 1)

            def tile(t, first=False, last=False):
                for kind, n in order_events(first, last):
                    if kind == "whigh":
                        high_weights(n)
                    elif kind == "duo" and n >= 0:
                        high_duo(t, n, first)
                    elif kind == "duo":
                        high_duo(t + 1, n + DUOS, False)
                    elif kind == "split":
                        spread_duo(*((t, n) if n >= 0 else (t + 1, n + DUOS)))
                    elif kind == "zout":
                        z_tile(t, n) if n >= 0 else z_tile(t - 1, KTILES - 1)
                    elif kind == "mlp":
                        mlp(t - 1, n, loop_bank(n))

            act.sem_inc(mlp_act, 1)
            tile(0, first=True)
            act.wait_ge(mlp_in, 5 * 16)
            with act.Fori(1, TILES - 1) as t:
                tile(t)
            tile(TILES - 1, last=True)
            z_tile(TILES - 1, KTILES - 1)
            for n in range(MLP_STEPS):
                mlp(TILES - 1, n, final_bank(n))


def kernel(**inputs):
    import numpy as np
    import concourse.bacc as bacc
    from concourse.bass_utils import run_bass_kernel_spmd

    nc = bacc.Bacc("TRN2", target_bir_lowering=False, num_devices=1)

    const = np.zeros((P, P + 62 + 32 * ROUND), np.float32)
    const[:, :P] = np.eye(P, dtype=np.float32)
    const[:EMBED, P + 30] = 1
    const[EMBED:, P + 31] = 1
    for f in range(CTX):
        g, n = divmod(f, CTX // ROUND)
        const[f, P + 62 + 32 * g + CTX_COL + n] = 1

    a = {k: np.asarray(v) for k, v in inputs.items()}
    arrays = {
        "const": const,
        "ids": a["ids"].reshape(TILES, SUBS, P, FIELDS).transpose(0, 2, 3, 1).reshape(TILES, P, FIELDS * SUBS),
        "w": a["L0_rec_w"].transpose(1, 0, 2).reshape(EMBED, PAIRS * EMBED),
        "w1": a["W_top1"][w1_rows()].reshape(KTILES, P, HID1).transpose(1, 0, 2),
        "w2": a["W_top2"].reshape(HID1 // P, P, HID2).transpose(1, 0, 2),
        "w3": a["W_top3"].reshape(HID2 // P, P).T,
        "b1": a["b_top1"].reshape(HID1 // P, P).T,
        "b2": a["b_top2"].reshape(HID2 // P, P).T,
        "ctx": a["dense_ctx"].T,
    }
    for f in range(FIELDS):
        arrays[f"tbl_{f}"] = a[f"tbl_{f}"]
    arrays = {f"in_{k}": np.ascontiguousarray(v) for k, v in arrays.items()}
    ap = {k: nc.dram_tensor(k, v.shape, mybir.dt.from_np(v.dtype), kind="ExternalInput").ap()
          for k, v in arrays.items()}
    out = nc.dram_tensor("out_y", (1, BATCH), mybir.dt.float32, kind="ExternalOutput").ap()
    dlrm_tower(nc, ap["in_const"], ap["in_ids"], ap["in_w"], ap["in_w1"], ap["in_w2"], ap["in_w3"], ap["in_b1"],
               ap["in_b2"], ap["in_ctx"], [ap[f"in_tbl_{f}"] for f in range(FIELDS)], out)
    r = run_bass_kernel_spmd(nc, [arrays], core_ids=[0])
    return r.results[0]["out_y"].reshape(BATCH, 1)
```
